# Optimizing a Trainium2 kernel written in Bass

```python
import numpy as np
import jax
import jax.numpy as jnp

def _softmax(x, axis=-1):
    return jax.nn.softmax(x, axis=axis)

def _gelu(x):
    return jax.nn.gelu(x, approximate=True)

def _silu(x):
    return jax.nn.silu(x)

def _sigmoid(x):
    return jax.nn.sigmoid(x)

def _layernorm(x, axis=-1, eps=1e-05):
    m = jnp.mean(x, axis=axis, keepdims=True)
    v = jnp.var(x, axis=axis, keepdims=True)
    return (x - m) / jnp.sqrt(v + eps)

def _scatter_add(tgt, idx, src, axis=0):
    return tgt.at[idx].add(src)

def _segment_sum(src, seg, n):
    return jax.ops.segment_sum(src, seg, n)
kernel_name = 'mk_perceiver_d1_seqx_r4_4f9493'

def setup_inputs(seed: int=0):
    np.random.seed(seed)
    _w = jnp.asarray

    def _rec_inputs():
        import jax
        import jax.numpy as jnp
        _rk = jax.random.key(seed)
        x = -0.0002928 + 1 * jax.random.normal(jax.random.fold_in(_rk, 1), (8, 64, 1024), jnp.float32)
        _lenS = 64 - jax.random.randint(jax.random.fold_in(_rk, 7), (8,), 0, max(1, 64 // 4) + 1, jnp.int32)
        _lenS2 = 256 - jax.random.randint(jax.random.fold_in(_rk, 8), (8,), 0, max(1, 256 // 4) + 1, jnp.int32)
        _ctx_4096P = jax.random.normal(jax.random.fold_in(_rk, 11), (8, 16, 1024), jnp.float32)
        _ctx_4096c = jax.random.dirichlet(jax.random.fold_in(_rk, 511), 0.3 * jnp.ones((16,), jnp.float32), (8, 256))
        _ctx_4096t = jnp.einsum('bsk,bkd->bsd', _ctx_4096c, _ctx_4096P)
        _ctx_4096t = _ctx_4096t * jax.lax.rsqrt(jnp.mean(jnp.square(_ctx_4096t)) + 1e-12) * 0.953939
        ctx_4096 = -2.8382e-05 + 0.999851 * (_ctx_4096t + 0.3 * jax.random.normal(jax.random.fold_in(_rk, 611), (8, 256, 1024), jnp.float32))
        _validS = jnp.arange(64)[None, :] < _lenS[:, None]
        _validS2 = jnp.arange(256)[None, :] < _lenS2[:, None]
        _causal = jnp.tril(jnp.ones((64, 64), dtype=bool))
        mask_1x1xSxS2_ff0 = jnp.where(jnp.ones((1, 1, 64, 256), dtype=bool), 0.0, -1000000000.0).astype(jnp.float32)
        return (x, ctx_4096, mask_1x1xSxS2_ff0)
    x, ctx_4096, mask_1x1xSxS2_ff0 = _rec_inputs()

    def _L0_xattn_setup():
        import jax, jax.numpy as jnp
        import numpy as np
        NUM_HEADS = 32
        NUM_KV_HEADS = 8
        HEAD_DIM = 128
        HIDDEN = 1024
        EPS = 1e-05

        def rmsnorm(x, w, eps=EPS):
            xf = x.astype(jnp.float32)
            var = jnp.mean(xf * xf, axis=-1, keepdims=True)
            return w * (xf * jax.lax.rsqrt(var + eps)).astype(x.dtype)
        key = jax.random.key(seed)
        ks = jax.random.split(key, 10)
        B, Q, KV = (1, 256, 1601)
        s = 1.0 / np.sqrt(HIDDEN)
        return {'hidden_states': jax.random.normal(ks[0], (B, Q, HIDDEN), jnp.float32), 'cross_attention_states': jax.random.normal(ks[1], (B, KV, HIDDEN), jnp.float32), 'attention_mask': jnp.zeros((B, 1, Q, KV), jnp.float32), 'q_proj_w': jax.random.normal(ks[2], (NUM_HEADS * HEAD_DIM, HIDDEN), jnp.float32) * s, 'k_proj_w': jax.random.normal(ks[3], (NUM_KV_HEADS * HEAD_DIM, HIDDEN), jnp.float32) * s, 'v_proj_w': jax.random.normal(ks[4], (NUM_KV_HEADS * HEAD_DIM, HIDDEN), jnp.float32) * s, 'o_proj_w': jax.random.normal(ks[5], (HIDDEN, NUM_HEADS * HEAD_DIM), jnp.float32) * s, 'q_norm_w': jnp.ones((HEAD_DIM,), jnp.float32), 'k_norm_w': jnp.ones((HEAD_DIM,), jnp.float32)}
    _L0_xattn_all = _L0_xattn_setup()
    _L0_xattn_in = {k: v for k, v in _L0_xattn_all.items() if k in ('q_proj_w', 'k_proj_w', 'v_proj_w', 'o_proj_w', 'q_norm_w', 'k_norm_w')}
    del _L0_xattn_all

    def _L0_attn_setup():
        import math
        import jax, jax.numpy as jnp
        import numpy as np
        B, T, E = (2, 512, 1024)
        H, HKV = (32, 8)
        DH = E // H
        G = H // HKV
        ROPE_THETA = 500000.0
        ROPE_FACTOR = 32.0
        HI_FREQ_FACTOR = 4.0
        LO_FREQ_FACTOR = 1.0
        ORIG_CTX = 2048

        def _rope_cos_sin(t_len):
            inv_freq = 1.0 / ROPE_THETA ** (jnp.arange(0, DH, 2, dtype=jnp.float32) / DH)
            wavelen = 2.0 * math.pi / inv_freq
            cut_lo = ORIG_CTX / HI_FREQ_FACTOR
            cut_hi = ORIG_CTX / LO_FREQ_FACTOR
            inv_freq = jnp.where(wavelen > cut_hi, inv_freq / ROPE_FACTOR, inv_freq)
            smooth = (ORIG_CTX / wavelen - LO_FREQ_FACTOR) / (HI_FREQ_FACTOR - LO_FREQ_FACTOR)
            smoothed = (1.0 - smooth) * inv_freq / ROPE_FACTOR + smooth * inv_freq
            is_medium = ~(wavelen < cut_hi) & ~(wavelen > cut_lo)
            inv_freq = jnp.where(is_medium, smoothed, inv_freq)
            pos = jnp.arange(t_len, dtype=jnp.float32)
            freqs = pos[:, None] * inv_freq[None, :]
            emb = jnp.concatenate([freqs, freqs], axis=-1)
            return (jnp.cos(emb), jnp.sin(emb))

        def _rotate_half(x):
            x1, x2 = jnp.split(x, 2, axis=-1)
            return jnp.concatenate([-x2, x1], axis=-1)
        key = jax.random.key(seed)
        kx, kq, kk, kv, ko = jax.random.split(key, 5)
        w = lambda k, shape: jax.random.normal(k, shape, jnp.float32) * 0.02
        return {'x': jax.random.normal(kx, (B, T, E), jnp.float32), 'Wq': w(kq, (E, E)), 'Wk': w(kk, (HKV * DH, E)), 'Wv': w(kv, (HKV * DH, E)), 'Wo': w(ko, (E, E))}
    _L0_attn_all = _L0_attn_setup()
    _L0_attn_in = {k: v for k, v in _L0_attn_all.items() if k in ('Wq', 'Wk', 'Wv', 'Wo')}
    del _L0_attn_all

    def _L0_ffn_setup():
        import jax, jax.numpy as jnp
        import numpy as np
        N_STREAMS = 4
        DIM = 256
        SINKHORN_ITERS = 50
        SINKHORN_TAU = 0.1
        RMS_EPS = 1.1920929e-07

        def sinkhorn_log(logits, num_iters=SINKHORN_ITERS, tau=SINKHORN_TAU):
            Z = logits / tau
            u0 = jnp.zeros(Z.shape[:-1], Z.dtype)
            v0 = jnp.zeros_like(u0)

            def step(carry, _):
                u, v = carry
                u = -jax.nn.logsumexp(Z + v[..., None, :], axis=-1)
                v = -jax.nn.logsumexp(Z + u[..., :, None], axis=-2)
                return ((u, v), None)
            (u, v), _ = jax.lax.scan(step, (u0, v0), None, length=num_iters)
            return jnp.exp(Z + u[..., :, None] + v[..., None, :])
        key = jax.random.key(seed)
        ks = jax.random.split(key, 6)
        B, T = (4, 512)
        n, C = (N_STREAMS, DIM)
        wd = n * C
        x = jax.random.normal(ks[0], (B, T, wd), dtype=jnp.float32)
        W_res = 0.01 * jax.random.normal(ks[1], (n * n, wd), dtype=jnp.float32)
        W_pre = 0.01 * jax.random.normal(ks[2], (n, wd), dtype=jnp.float32)
        W_post = 0.01 * jax.random.normal(ks[3], (n, wd), dtype=jnp.float32)
        H_res_base = jnp.full((n, n), -0.5, dtype=jnp.float32)
        H_res_base = H_res_base.at[jnp.arange(n), jnp.arange(n)].set(0.0)
        H_pre_base = jnp.zeros((n,), dtype=jnp.float32).at[0].set(1.0)
        H_post_base = jnp.zeros((n,), dtype=jnp.float32)
        gate = jnp.array([5.0], dtype=jnp.float32)
        W_branch = 1.0 / np.sqrt(C) * jax.random.normal(ks[4], (C, C), dtype=jnp.float32)
        return {'x': x, 'W_res': W_res, 'W_pre': W_pre, 'W_post': W_post, 'H_res_base': H_res_base, 'H_pre_base': H_pre_base, 'H_post_base': H_post_base, 'gate': gate, 'W_branch': W_branch}
    _L0_ffn_all = _L0_ffn_setup()
    _L0_ffn_in = {k: v for k, v in _L0_ffn_all.items() if k in ('W_res', 'W_pre', 'W_post', 'H_res_base', 'H_pre_base', 'H_post_base', 'gate', 'W_branch')}
    del _L0_ffn_all
    return {'x': x, 'ctx_4096': ctx_4096, 'mask_1x1xSxS2_ff0': mask_1x1xSxS2_ff0, 'L0_xattn_q_proj_w': _L0_xattn_in['q_proj_w'], 'L0_xattn_k_proj_w': _L0_xattn_in['k_proj_w'], 'L0_xattn_v_proj_w': _L0_xattn_in['v_proj_w'], 'L0_xattn_o_proj_w': _L0_xattn_in['o_proj_w'], 'L0_xattn_q_norm_w': _L0_xattn_in['q_norm_w'], 'L0_xattn_k_norm_w': _L0_xattn_in['k_norm_w'], 'L0_attn_Wq': _L0_attn_in['Wq'], 'L0_attn_Wk': _L0_attn_in['Wk'], 'L0_attn_Wv': _L0_attn_in['Wv'], 'L0_attn_Wo': _L0_attn_in['Wo'], 'L0_ffn_W_res': _L0_ffn_in['W_res'], 'L0_ffn_W_pre': _L0_ffn_in['W_pre'], 'L0_ffn_W_post': _L0_ffn_in['W_post'], 'L0_ffn_H_res_base': _L0_ffn_in['H_res_base'], 'L0_ffn_H_pre_base': _L0_ffn_in['H_pre_base'], 'L0_ffn_H_post_base': _L0_ffn_in['H_post_base'], 'L0_ffn_gate': _L0_ffn_in['gate'], 'L0_ffn_W_branch': _L0_ffn_in['W_branch']}

def reference(x, ctx_4096, mask_1x1xSxS2_ff0, L0_xattn_q_proj_w, L0_xattn_k_proj_w, L0_xattn_v_proj_w, L0_xattn_o_proj_w, L0_xattn_q_norm_w, L0_xattn_k_norm_w, L0_attn_Wq, L0_attn_Wk, L0_attn_Wv, L0_attn_Wo, L0_ffn_W_res, L0_ffn_W_pre, L0_ffn_W_post, L0_ffn_H_res_base, L0_ffn_H_pre_base, L0_ffn_H_post_base, L0_ffn_gate, L0_ffn_W_branch):
    import jax
    import jax.numpy as jnp

    def _L0_xattn_ref(hidden_states, cross_attention_states, attention_mask, q_proj_w, k_proj_w, v_proj_w, o_proj_w, q_norm_w, k_norm_w):
        import jax, jax.numpy as jnp
        import numpy as np
        NUM_HEADS = 32
        NUM_KV_HEADS = 8
        HEAD_DIM = 128
        HIDDEN = 1024
        EPS = 1e-05

        def rmsnorm(x, w, eps=EPS):
            xf = x.astype(jnp.float32)
            var = jnp.mean(xf * xf, axis=-1, keepdims=True)
            return w * (xf * jax.lax.rsqrt(var + eps)).astype(x.dtype)
        B, Q, _ = hidden_states.shape
        KV = cross_attention_states.shape[1]
        n_rep = NUM_HEADS // NUM_KV_HEADS
        q = (hidden_states @ q_proj_w.T).reshape(B, Q, NUM_HEADS, HEAD_DIM).transpose(0, 2, 1, 3)
        k = (cross_attention_states @ k_proj_w.T).reshape(B, KV, NUM_KV_HEADS, HEAD_DIM).transpose(0, 2, 1, 3)
        v = (cross_attention_states @ v_proj_w.T).reshape(B, KV, NUM_KV_HEADS, HEAD_DIM).transpose(0, 2, 1, 3)
        q = rmsnorm(q, q_norm_w)
        k = jnp.repeat(k, n_rep, axis=1)
        v = jnp.repeat(v, n_rep, axis=1)
        k = rmsnorm(k, k_norm_w)
        scale = 1.0 / np.sqrt(HEAD_DIM)
        scores = jnp.einsum('bhqd,bhkd->bhqk', q, k) * scale + attention_mask
        attn = jax.nn.softmax(scores.astype(jnp.float32), axis=-1).astype(q.dtype)
        out = jnp.einsum('bhqk,bhkd->bhqd', attn, v)
        out = out.transpose(0, 2, 1, 3).reshape(B, Q, NUM_HEADS * HEAD_DIM)
        return out @ o_proj_w.T

    def _L0_attn_ref(x, Wq, Wk, Wv, Wo):
        import math
        import jax, jax.numpy as jnp
        import numpy as np
        B, T, E = (2, 512, 1024)
        H, HKV = (32, 8)
        DH = E // H
        G = H // HKV
        ROPE_THETA = 500000.0
        ROPE_FACTOR = 32.0
        HI_FREQ_FACTOR = 4.0
        LO_FREQ_FACTOR = 1.0
        ORIG_CTX = 2048

        def _rope_cos_sin(t_len):
            inv_freq = 1.0 / ROPE_THETA ** (jnp.arange(0, DH, 2, dtype=jnp.float32) / DH)
            wavelen = 2.0 * math.pi / inv_freq
            cut_lo = ORIG_CTX / HI_FREQ_FACTOR
            cut_hi = ORIG_CTX / LO_FREQ_FACTOR
            inv_freq = jnp.where(wavelen > cut_hi, inv_freq / ROPE_FACTOR, inv_freq)
            smooth = (ORIG_CTX / wavelen - LO_FREQ_FACTOR) / (HI_FREQ_FACTOR - LO_FREQ_FACTOR)
            smoothed = (1.0 - smooth) * inv_freq / ROPE_FACTOR + smooth * inv_freq
            is_medium = ~(wavelen < cut_hi) & ~(wavelen > cut_lo)
            inv_freq = jnp.where(is_medium, smoothed, inv_freq)
            pos = jnp.arange(t_len, dtype=jnp.float32)
            freqs = pos[:, None] * inv_freq[None, :]
            emb = jnp.concatenate([freqs, freqs], axis=-1)
            return (jnp.cos(emb), jnp.sin(emb))

        def _rotate_half(x):
            x1, x2 = jnp.split(x, 2, axis=-1)
            return jnp.concatenate([-x2, x1], axis=-1)
        b, t, _ = x.shape
        q = (x @ Wq.T).reshape(b, t, H, DH).transpose(0, 2, 1, 3)
        k = (x @ Wk.T).reshape(b, t, HKV, DH).transpose(0, 2, 1, 3)
        v = (x @ Wv.T).reshape(b, t, HKV, DH).transpose(0, 2, 1, 3)
        cos, sin = _rope_cos_sin(t)
        cos = cos.astype(x.dtype)[None, None]
        sin = sin.astype(x.dtype)[None, None]
        q = q * cos + _rotate_half(q) * sin
        k = k * cos + _rotate_half(k) * sin
        qg = q.reshape(b, HKV, G, t, DH)
        scores = jnp.einsum('bhgtd,bhkd->bhgtk', qg.astype(jnp.float32), k.astype(jnp.float32)) / math.sqrt(DH)
        causal = jnp.tril(jnp.ones((t, t), dtype=bool))
        scores = jnp.where(causal[None, None, None], scores, jnp.finfo(jnp.float32).min)
        attn = jax.nn.softmax(scores, axis=-1).astype(x.dtype)
        ctx = jnp.einsum('bhgtk,bhkd->bhgtd', attn, v)
        out = ctx.reshape(b, H, t, DH).transpose(0, 2, 1, 3).reshape(b, t, E)
        return out @ Wo.T

    def _L0_ffn_ref(x, W_res, W_pre, W_post, H_res_base, H_pre_base, H_post_base, gate, W_branch):
        import jax, jax.numpy as jnp
        import numpy as np
        N_STREAMS = 4
        DIM = 256
        SINKHORN_ITERS = 50
        SINKHORN_TAU = 0.1
        RMS_EPS = 1.1920929e-07

        def sinkhorn_log(logits, num_iters=SINKHORN_ITERS, tau=SINKHORN_TAU):
            Z = logits / tau
            u0 = jnp.zeros(Z.shape[:-1], Z.dtype)
            v0 = jnp.zeros_like(u0)

            def step(carry, _):
                u, v = carry
                u = -jax.nn.logsumexp(Z + v[..., None, :], axis=-1)
                v = -jax.nn.logsumexp(Z + u[..., :, None], axis=-2)
                return ((u, v), None)
            (u, v), _ = jax.lax.scan(step, (u0, v0), None, length=num_iters)
            return jnp.exp(Z + u[..., :, None] + v[..., None, :])
        B, T, nC = x.shape
        n = N_STREAMS
        C = nC // n
        x_norm = x * jax.lax.rsqrt(jnp.mean(x * x, axis=-1, keepdims=True) + RMS_EPS)
        H_res_logits = (x_norm @ W_res.T).reshape(B, T, n, n) + H_res_base
        H_pre_logits = x_norm @ W_pre.T + H_pre_base
        H_post_logits = x_norm @ W_post.T + H_post_base
        H_res = sinkhorn_log(H_res_logits)
        H_pre = jax.nn.softmax(H_pre_logits, axis=-1)
        H_post = jax.nn.softmax(H_post_logits, axis=-1)
        g = jax.nn.sigmoid(gate)[0]
        I = jnp.eye(n, dtype=H_res.dtype)
        H_res = (1.0 - g) * I + g * H_res
        x_streams = x.reshape(B, T, n, C)
        x_pre = jnp.einsum('btnc,btn->btc', x_streams, H_pre)
        y = x_pre @ W_branch
        x_mixed = jnp.einsum('btij,btjc->btic', H_res, x_streams)
        y_distributed = jnp.einsum('btc,btn->btnc', y, H_post)
        return (x_mixed + y_distributed).reshape(B, T, nC)
    x = x + _L0_xattn_ref(_layernorm(x, axis=-1), ctx_4096, mask_1x1xSxS2_ff0, L0_xattn_q_proj_w, L0_xattn_k_proj_w, L0_xattn_v_proj_w, L0_xattn_o_proj_w, L0_xattn_q_norm_w, L0_xattn_k_norm_w)
    x = x + _L0_attn_ref(_layernorm(x, axis=-1), L0_attn_Wq, L0_attn_Wk, L0_attn_Wv, L0_attn_Wo)
    x = x + _L0_ffn_ref(_layernorm(x, axis=-1), L0_ffn_W_res, L0_ffn_W_pre, L0_ffn_W_post, L0_ffn_H_res_base, L0_ffn_H_pre_base, L0_ffn_H_post_base, L0_ffn_gate, L0_ffn_W_branch)
    return x

_drawn_inputs = setup_inputs


def setup_inputs(seed=0):
    import zlib

    import numpy as np

    out = dict(_drawn_inputs(seed))
    spreads = {'L0_xattn_q_norm_w': (1.0, 0.2),
     'L0_xattn_k_norm_w': (1.0, 0.2),
     'L0_ffn_H_post_base': (0.0, 0.8)}
    factors = {'L0_attn_Wq': 3.461, 'L0_attn_Wk': 3.137, 'L0_ffn_W_pre': 3.84, 'L0_ffn_W_post': 3.077}
    for name, (base, spread) in spreads.items():
        noise = np.random.default_rng([zlib.crc32(name.encode()), seed]).standard_normal(out[name].shape)
        drawn = base * np.exp(spread * noise) if base else spread * noise
        out[name] = jnp.asarray(drawn.astype(out[name].dtype))
    for name, factor in factors.items():
        out[name] = (out[name] * factor).astype(out[name].dtype)
    return out
```

```python
from contextlib import ExitStack

import concourse.bass as bass
from concourse import mybir

F32 = mybir.dt.float32
F32R = mybir.dt.float32r
ALU = mybir.AluOpType
ACT = mybir.ActivationFunctionType
AX = mybir.AxisListType.X

P = 128
B, S, E = 8, 64, 1024
SC = 256
NH, NKV, DH = 32, 8, 128
NT = B * S // P
NC = E // P
UW = 512
GPU = NC
DS = 32
ROW = 4
NSTR, CW = 4, 256
ITERS, EPOCH = 50, 10
EPS = 1e-5
EPS_FFN = 1.1920929e-07
TAU_INV = float(1.0 / 0.10000000149011612)

M_UNIT0 = 8
M_CTX0 = M_UNIT0 + 10 * GPU
M_IT0 = M_CTX0 + 4
M_IT1 = M_IT0 + 8
M_W1 = M_IT1 + 7 * 12
M_IT8 = M_W1 + 2 * GPU
M_IT15 = M_IT8 + 7 * 12
M_TAIL = M_IT15 + 8
M_O1 = M_TAIL + 4 + GPU
M_LN2 = M_O1 + 7 * GPU + GPU
M_U21 = M_LN2 + 8


def perceiver(nc, x, ctx_in, mask_x, wq1, wk1, wv1, wo1, qn_w, kn_w, wq2, wk2, wv2, wo2,
              w_res, w_pre, w_post, res_base, pre_base, post_base, gate, w_branch,
              ident_in, cos_in, sin_in, causal_in, q_rows, ot_hi, ot_lo, out):
    es = ExitStack()

    def sb(name, shape, dt=F32):
        return es.enter_context(nc.sbuf_tensor(name, shape, dt))

    def sem(name):
        return es.enter_context(nc.semaphore(name))

    with es:
        wt = sb("wt", [P, 2, 2, NC, UW], F32R)
        act = sb("act", [P, 2, 2, 4096], F32R)
        ctxT = [act[:, 0, p, 0:2048].rearrange("p (c k) -> p c k", c=NC) for p in range(2)]
        s1 = [act[:, 1, p, :] for p in range(2)]
        kT = [s1[p][:, 0:1024].rearrange("p (g k) -> p g k", g=4) for p in range(2)]
        vN = [s1[p][:, 1024:2048].rearrange("p (t n) -> p t n", t=2) for p in range(2)]
        qT = [s1[p][:, 2048:3072] for p in range(2)]
        pT = [s1[p][:, 3072:3584] for p in range(2)]
        oS = [s1[p][:, 3584:4096].rearrange("p (s n) -> p s n", s=2) for p in range(2)]
        raw = sb("raw", [P, 2, 4, E])
        xr = sb("xr", [P, NT, E])
        ctxN = xr[:, 0:2, :]
        qN = xr[:, 2, :]
        G = sb("G", [P, 7168])
        hb = [G[:, 0:1024], G[:, 1024:2048]]
        qst = [G[:, 2048 + 512 * t:2560 + 512 * t] for t in range(4)]
        kn = [G[:, 512 * t:512 * t + 512] for t in range(2)]
        sqk = G[:, 1024:1536]
        sqq = G[:, 1536:2560]
        sT = G[:, 2560:3072]
        pN = G[:, 3072:3584]
        mask2 = G[:, 3584:3840]
        kT4 = G[:, 0:4096].rearrange("p (g n) -> p g n", g=8)
        vS = G[:, 4096:5120].rearrange("p (t n) -> p t n", t=NT)
        qr = [G[:, 5120:5632], G[:, 5632:6144]]
        kr4 = G[:, 5120:6144].rearrange("p (g r d) -> p g r d", g=8, r=4)
        t2 = G[:, 6144:6656]
        cosb = G[:, 6656:6688]
        sinb = G[:, 6688:6720]
        cmask = G[:, 6720:6976]
        q2T = raw[:, 1, :, :].rearrange("p a b -> p (a b)").rearrange("p (g n) -> p g n", g=8)
        raw0 = raw[:, 0, :, :].rearrange("p a b -> p (a b)")
        raw1 = raw[:, 1, :, :].rearrange("p a b -> p (a b)")
        s2 = [raw0[:, 0:1024], raw0[:, 1024:2048]]
        pT2 = G[:, 4096:5120].rearrange("p (h m n) -> p h m n", h=4, m=2)
        vD = raw0[:, 2048:4096].rearrange("p (b n) -> p b n", b=B)
        z = G[:, 0:4096].rearrange("p (t n) -> p t n", t=NT)
        w24 = G[:, 5120:6144]
        w24T = G[:, 6976:7168].rearrange("p (c n) -> p c n", c=NC)
        yS = raw0.rearrange("p (t n) -> p t n", t=NT)
        wb = G[:, 6144:6656].rearrange("p (c n) -> p c n", c=2)
        zT = [raw1[:, 1024 * t:1024 * t + 1024].rearrange("p (c n) -> p c n", c=NC) for t in range(2)]
        zsq = raw1[:, 2048:3072]
        xp = [raw1[:, 3072 + 256 * t:3328 + 256 * t] for t in range(2)]
        xpT = [raw1[:, 3584 + 256 * t:3840 + 256 * t].rearrange("p (c n) -> p c n", c=2) for t in range(2)]
        ident = sb("ident", [P, P])
        small = sb("small", [P, 640])
        col = [0]

        def cols(n):
            col[0] += n
            return small[:, col[0] - n:col[0]]

        qw, kw, wqk = cols(1), cols(1), cols(1)
        mhalf, epsd = cols(8), cols(8)
        bst, bag, lnv, lnr = cols(12), cols(8), cols(4), cols(4)
        ssk, msk, rk = cols(4), cols(4), cols(4)
        ssq, msq, rq = cols(8), cols(8), cols(8)
        nmx, sm, rsm = cols(16), cols(16), cols(16)
        ssz, msz, rz = cols(4), cols(4), cols(4)
        base24, gts = cols(24), cols(4)
        L = cols(96).rearrange("p (t n) -> p t n", t=NT)
        A = cols(64)
        Kx = cols(64)
        tk = cols(64)
        uv = cols(32)
        luv = cols(32)
        h8 = cols(32)
        h8m, h8s = cols(8), cols(8)
        hres = cols(64)
        assert col[0] <= 640

        ps = es.enter_context(nc.psum_tensor("ps", [P, 8, 512], F32))
        T = [ps[:, 0, :], ps[:, 1, :]]
        acc = [ps[:, 2 + t, :] for t in range(4)]
        kacc = [ps[:, 2, :], ps[:, 3, :]]
        vacc = [ps[:, 6, :], ps[:, 7, :]]
        sacc = ps[:, 4, :]
        oacc = ps[:, 5, 0:256]

        x_loaded, const_loaded = sem("x_loaded"), sem("const_loaded")
        mhalf_ready, ident_ready, mask_loaded = sem("mhalf_ready"), sem("ident_ready"), sem("mask_loaded")
        raw_loaded = [sem("raw_loaded0"), sem("raw_loaded1")]
        ctx_loaded, qn_loaded = sem("ctx_loaded"), sem("qn_loaded")
        act_loaded = [sem("act_loaded0"), sem("act_loaded1")]
        turned, hi_done, lo_done = sem("turned"), sem("hi_done"), sem("lo_done")
        ln_var, ln_rstd, ln_done = sem("ln_var"), sem("ln_rstd"), sem("ln_done")
        dv = sem("dv")
        acc_done, acc_free = sem("acc_done"), sem("acc_free")
        q_stored = sem("q_stored")
        k_done, k_squared, k_var, k_rstd, k_normed = (sem(n) for n in (
            "k_done", "k_squared", "k_var", "k_rstd", "k_normed"))
        v_done, v_hi, v_lo = sem("v_done"), sem("v_hi"), sem("v_lo")
        q_squared, q_summed, q_var, q_rstd = sem("q_squared"), sem("q_summed"), sem("q_var"), sem("q_rstd")
        k_summed, sum_inverted, wqk_ready = sem("k_summed"), sem("sum_inverted"), sem("wqk_ready")
        s_done, s_read, s_max, p_exp, p_normed = (sem(n) for n in (
            "s_done", "s_read", "s_max", "p_exp", "p_normed"))
        o_done, o_hi, o_lo = sem("o_done"), sem("o_hi"), sem("o_lo")
        o_stored = [sem("o_stored0"), sem("o_stored1")]
        x1_done = sem("x1_done")
        kv_roped, q_roped, t_done, t_read = sem("kv_roped"), sem("q_roped"), sem("t_done"), sem("t_read")
        v_doubled = sem("v_doubled")
        s2_done, s2_read, s2_ready, p2_exp, p2_normed, o2_done, o2_hi, o2_lo = (sem(n) for n in (
            "s2_done", "s2_read", "s2_ready", "p2_exp", "p2_normed", "o2_done", "o2_hi", "o2_lo"))
        mix_ready, z_squared, z_var, z_rstd = (sem(n) for n in (
            "mix_ready", "z_squared", "z_var", "z_rstd"))
        w24_loaded, w24_turned, w24_ready = sem("w24_loaded"), sem("w24_turned"), sem("w24_ready")
        f_done, f_ready, lg_done, lg_read, xp_done, y_done = (sem(n) for n in (
            "f_done", "f_ready", "lg_done", "lg_read", "xp_done", "y_done"))
        sk_in, sk_out, y_scaled, y_added, pl = (sem(n) for n in (
            "sk_in", "sk_out", "y_scaled", "y_added", "pl"))
        out_ready, out_stored = sem("out_ready"), sem("out_stored")

        def some(count):
            return not isinstance(count, int) or count > 0

        x_rows = x.rearrange("b s e -> (b s) e").rearrange("(t p) e -> p t e", p=P)
        out_rows = out.rearrange("b s e -> (b s) e").rearrange("(t p) e -> p t e", p=P)

        def unit_rows(n):
            def rows(w, r0, nb, c0=0):
                return w[r0:r0 + nb * P, c0:c0 + E].rearrange("(j p) e -> p j e", p=P)
            if n < 8:
                return [(0, 4, rows(wq1, n * UW, 4))]
            if n < 12:
                w = wk1 if n % 2 == 0 else wv1
                return [(0, 4, rows(w, (n - 8) // 2 * UW, 4))]
            if n < 20:
                o, k = divmod(n - 12, 4)
                return [(0, 4, rows(wo1, o * UW, 4, k * E))]
            if n == 20:
                return [(0, 2, rows(wk2, 0, 2)), (2, 2, rows(wv2, 0, 2))]
            if n < 23:
                return [(0, 4, rows(wq2, (n - 21) * UW, 4))]
            return [(0, 4, rows(wo2, (n - 23) * UW, 4))]

        def raw_slot(n):
            return n % 2 if n < 22 else 0

        raw_count = {}
        seen = [0, 0]
        for n in range(25):
            seen[raw_slot(n)] += 16 * (2 if n == 20 else 1)
            raw_count[n] = seen[raw_slot(n)]

        def groups_before(n):
            if n < 10:
                return M_UNIT0 + GPU * n
            if n < 12:
                return M_W1 + GPU * (n - 10)
            if n == 12:
                return M_TAIL
            if n < 20:
                return M_O1 + GPU * (n - 13)
            return {20: M_O1 + 7 * GPU, 21: M_U21, 22: M_U21 + 8, 23: M_U21 + 16, 24: M_U21 + 24}[n]

        def groups_after(n):
            return M_O1 if n == 12 else groups_before(n) + GPU

        block = es.enter_context(nc.Block())

        @block.sync
        def _(sp):
            def load_unit(n):
                for j, nb, rows in unit_rows(n):
                    sp.dma_start(raw[:, raw_slot(n), j:j + nb, :], rows).then_inc(raw_loaded[raw_slot(n)], 16)

            sp.dma_start(ident[:], ident_in).then_inc(ident_ready, 16)
            sp.dma_start(xr[:], x_rows).then_inc(x_loaded, 16)
            load_unit(0)
            load_unit(1)
            sp.dma_start(cosb, cos_in).then_inc(const_loaded, 16)
            sp.dma_start(sinb, sin_in).then_inc(const_loaded, 16)
            sp.dma_start(cmask, causal_in).then_inc(const_loaded, 16)
            sp.dma_start(qw, qn_w.rearrange("(d a) -> d a", a=1)).then_inc(const_loaded, 16)
            sp.dma_start(kw, kn_w.rearrange("(d a) -> d a", a=1)).then_inc(const_loaded, 16)
            for a, n, r in ((0, 16, res_base.rearrange("a b -> (a b)")), (16, 4, pre_base), (20, 4, post_base)):
                sp.dma_start(base24[:, a:a + n], r.partition_broadcast(P)).then_inc(const_loaded, 16)
            sp.dma_start(gts[:, 0:1], gate.partition_broadcast(P)).then_inc(const_loaded, 16)

            def store_queries(n, col_of, half, g):
                for t in range(NT):
                    sp.wait_ge(acc_free, col_of + t + 1)
                    for h2 in range(2):
                        src = qst[t].rearrange("p (j h d) -> p j h d", j=2, h=2)[:, :, h2, :]
                        dst = q_rows[half, h2, 2 * t:2 * t + 2].rearrange("b s g j d -> (b s) g j d")[:, g]
                        sp.dma_start(dst, src).then_inc(q_stored, 16)

            for n in range(8):
                sp.wait_ge(turned, groups_before(n) + GPU)
                load_unit(n + 2)
                store_queries(n, 4 * n, n // 4, n % 4)
            sp.wait_ge(ln_done, NT)
            sp.dma_start(ctxN, ctx_in[0].rearrange("(t p) e -> p t e", p=P)).then_inc(ctx_loaded, 16)
            for n in (8, 9):
                sp.wait_ge(turned, groups_before(n) + GPU)
                load_unit(n + 2)
            sp.wait_ge(q_stored, 8 * NT * 32)
            sp.dma_start(mask2[0:S, :], mask_x[0, 0]).then_inc(mask_loaded, 16)
            sp.dma_start(mask2[S:P, :], mask_x[0, 0]).then_inc(mask_loaded, 16)

            def load_ctx(b):
                sp.dma_start(ctxN, ctx_in[b].rearrange("(t p) e -> p t e", p=P)).then_inc(ctx_loaded, 16)

            def load_q(b, half):
                sp.dma_start(qN, q_rows[half, :, b].rearrange("h s g j d -> h s (g j d)")).then_inc(qn_loaded, 16)

            load_q(0, 0)
            sp.wait_ge(turned, M_IT0)
            load_ctx(1)

            def store_o(a, g, b, half):
                sp.wait_ge(o_lo, 4 * a + g + 1)
                for p, dst in enumerate((ot_hi, ot_lo)):
                    d = dst[:, half, 4 * g:4 * g + 4, b]
                    sp.dma_start(d, oS[p][:, g % 2, :].bitcast(F32).rearrange("p (h s) -> p h s", h=4)).then_inc(o_stored[g % 2], 16)

            def iteration(i, m, b_ctx, bq, hq, b_o, h_o, att=True, more=True):
                if att:
                    for g in range(3):
                        store_o(i - 1, g, b_o, h_o)
                if more is True:
                    sp.wait_ge(turned, m + (11 if att else 7))
                    load_ctx(b_ctx)
                if more is not None:
                    sp.wait_ge(hi_done, m + (12 if att else 8))
                    load_q(bq, hq)
                if att:
                    store_o(i - 1, 3, b_o, h_o)

            iteration(0, M_IT0, 2, 1, 0, 0, 0, att=False)
            iteration(1, M_IT1, 3, 2, 0, 0, 0)
            with sp.Fori(2, 6) as i:
                iteration(i, 12 * i + (M_IT1 - 12), i + 2, i + 1, 0, i - 1, 0)
            iteration(6, M_IT1 + 60, 0, 7, 0, 5, 0)
            iteration(7, M_IT1 + 72, 1, 0, 1, 6, 0)
            for n in (10, 11):
                sp.wait_ge(turned, groups_before(n) + GPU)
                load_unit(n + 2)
            iteration(8, M_IT8, 2, 1, 1, 7, 0)
            with sp.Fori(9, 14) as i:
                iteration(i, 12 * i + (M_IT8 - 96), i - 6, i - 7, 1, i - 9, 1)
            iteration(14, M_IT8 + 72, 0, 7, 1, 5, 1, more=False)
            iteration(15, M_IT15, 0, 0, 0, 6, 1, more=None)

            def load_quarter(n):
                k = (n - 12) % 4
                for p, src in enumerate((ot_hi, ot_lo)):
                    s = src[:, k // 2, (k % 2) * 8:(k % 2) * 8 + 8].rearrange("p h b s -> p (h b s)")
                    sp.dma_start(act[:, n % 2, p, :].bitcast(F32), s
                                 ).then_inc(act_loaded[n % 2], 16)

            sp.wait_ge(v_done, 32)
            load_quarter(12)
            sp.wait_ge(turned, M_IT15 + 10)
            sp.wait_ge(q_squared, 16)
            sp.dma_start(xr[:], x_rows).then_inc(x_loaded, 16)
            for g in range(4):
                store_o(15, g, 7, 1)
            sp.wait_ge(o_stored[0], 32 * 32)
            sp.wait_ge(o_stored[1], 32 * 32)
            sp.wait_ge(o_done, 64)
            load_quarter(13)
            for n in range(12, 20):
                sp.wait_ge(turned, groups_after(n))
                load_unit(n + 2)
                if n + 2 < 20:
                    sp.wait_ge(acc_done, 32 + 4 * (n - 12) + 4)
                    load_quarter(n + 2)
            sp.wait_ge(turned, groups_after(20))
            load_unit(22)
            sp.wait_ge(turned, groups_after(22))
            load_unit(23)
            sp.wait_ge(turned, groups_after(23))
            for t2_ in range(2):
                for dup in range(2):
                    dst = vD.rearrange("p (t b) n -> p t b n", b=2)[dup * S:(dup + 1) * S, :, t2_, :]
                    sp.dma_start(dst, vS[t2_ * S:(t2_ + 1) * S]).then_inc(v_doubled, 16)
            sp.wait_ge(q_roped, 8)
            sp.dma_start(wb, w_branch.rearrange("(c p) n -> p c n", p=P)).then_inc(w24_loaded, 16)
            sp.wait_ge(t_done, 16)
            for a, n, w in ((0, 16, w_res), (16, 4, w_pre), (20, 4, w_post)):
                sp.dma_start(w24[a:a + n, :], w).then_inc(w24_loaded, 16)
            sp.wait_ge(o2_done, 8)
            load_unit(24)
            for t in range(NT):
                sp.wait_ge(out_ready, t + 1)
                sp.dma_start(out_rows[:, t, :], xr[:, t, :]).then_inc(out_stored, 16)
            sp.wait_ge(out_stored, 16 * NT)

        @block.tensor
        def _(pe):
            def turn(m, par, blocks):
                if some(m - 1):
                    pe.wait_ge(lo_done, m - 1)
                for j, src in enumerate(blocks):
                    tr = pe.transpose(T[par][:, j * P:(j + 1) * P], src, ident[:])
                tr.then_inc(turned, 1)

            def turn_unit(slot, g, m, arrived):
                if g == 0:
                    pe.wait_ge(raw_loaded[slot], arrived)
                turn(m, g % 2, [raw[:, slot, j, g * P:(g + 1) * P] for j in range(4)])

            def turn_unit_n(n, g):
                turn_unit(raw_slot(n), g, groups_before(n) + g, raw_count[n])

            def products(n_slot, lhs, before, after, acc_from=True, acc_to=True, between=None):
                for t in range(NT):
                    before(t)
                    for q in range(3 * NC):
                        c, p = divmod(q, 3)
                        mm = pe.matmul(acc[t], lhs(p == 2, c, t), wt[:, n_slot, int(p == 1), c, :],
                                       start=(acc_from and q == 0), stop=(acc_to and q == 3 * NC - 1))
                        if q == 11 and between:
                            between(2 * t)
                    after(t, mm)
                    if between:
                        between(2 * t + 1)

            def lhs_of(slot):
                return lambda lo, c, t: act[:, slot, int(lo), c * UW + t * P:c * UW + (t + 1) * P]

            pe.wait_ge(ident_ready, 16)
            for t in range(NT):
                pe.wait_ge(ln_done, t + 1)
                for g in range(2):
                    turn(2 * t + g, g, [hb[t % 2][:, (4 * g + j) * P:(4 * g + j + 1) * P] for j in range(4)])
            for g in range(GPU):
                turn_unit_n(0, g)

            def query_unit(n, par):
                pe.wait_ge(lo_done, M_UNIT0 + GPU + GPU * n)

                def before(t):
                    if some(4 * n - 3 + t):
                        pe.wait_ge(acc_free, 4 * n - 3 + t)

                def after(t, mm):
                    mm.then_inc(acc_done, 1)

                arrived = 8 * (n + par) + 16

                def between(k):
                    turn_unit(1 - par, k, M_UNIT0 + GPU + GPU * n + k, arrived)
                products(par, lhs_of(0), before, after, between=between)

            query_unit(0, 0)
            query_unit(1, 1)
            with pe.Fori(1, 4) as i2:
                query_unit(2 * i2, 0)
                query_unit(2 * i2 + 1, 1)
            for g in range(GPU):
                turn_unit_n(9, g)

            def ctx_blocks(kt, g):
                return [ctxN[:, kt, (4 * g + j) * P:(4 * g + j + 1) * P] for j in range(4)]

            pe.wait_ge(ctx_loaded, 16)
            for kt in range(2):
                for g in range(2):
                    turn(M_CTX0 + 2 * kt + g, g, ctx_blocks(kt, g))

            def project(bank, kt, slot, q0, q1):
                for q in range(q0, q1):
                    c, p = divmod(q, 3)
                    mm = pe.matmul(bank, ctxT[int(p == 2)][:, c, kt * P:(kt + 1) * P],
                                   wt[:, slot, int(p == 1), c, :], start=(q == 0), stop=(q == 3 * NC - 1))
                return mm

            def scores(a, g):
                if some(4 * a + g):
                    pe.wait_ge(s_read, 4 * a + g)
                for j in range(2):
                    lhs = [qT[p][:, (2 * g + j) * P:(2 * g + j + 1) * P] for p in range(2)]
                    for p, r in ((0, 0), (0, 1), (1, 0)):
                        mm = pe.matmul(sacc[:, j * 256:(j + 1) * 256], lhs[p], kT[r][:, g, :],
                                       start=(p == 0 and r == 0), stop=(p == 1))
                mm.then_inc(s_done, 1)

            def turn_probs(a, g, m, par):
                pe.wait_ge(p_normed, 4 * a + g + 1)
                turn(m, par, [pN[:, j * 256 + kt * P:j * 256 + (kt + 1) * P] for kt in range(2) for j in range(2)])

            def weigh(a, g, m):
                pe.wait_ge(lo_done, m + 1)
                if some(4 * a + g):
                    pe.wait_ge(o_lo, 4 * a + g)
                n = 0
                for kt in range(2):
                    for r, p in ((0, 0), (0, 1), (1, 0)):
                        mm = pe.matmul(oacc, vN[r][:, kt, g * P:(g + 1) * P], pT[p][:, kt * 256:(kt + 1) * 256],
                                       start=(n == 0), stop=(n == 5))
                        n += 1
                mm.then_inc(o_done, 1)

            def turn_k(i, kt, m, par):
                pe.wait_ge(k_normed, 2 * i + kt + 1)
                turn(m, par, [kn[kt][:, g * P:(g + 1) * P] for g in range(4)])

            def turn_q(i, half, m, par):
                if half == 0:
                    pe.wait_ge(qn_loaded, 16 * (i + 1))
                turn(m, par, [qN[:, (4 * half + j) * P:(4 * half + j + 1) * P] for j in range(4)])

            def turn_ctx(i, kt, m):
                if kt == 0:
                    pe.wait_ge(ctx_loaded, 16 * (i + 2))
                turn(m, 0, ctx_blocks(kt, 0))
                turn(m + 1, 1, ctx_blocks(kt, 1))

            def iteration(i, m, att=True, more=True):
                a = i - 1
                pe.wait_ge(lo_done, m - 1)
                if some(2 * i - 1):
                    pe.wait_ge(k_normed, 2 * i - 1)
                if isinstance(i, int) and i == 0:
                    pe.wait_ge(acc_free, 32)
                mm = project(kacc[0], 0, 0, 0, 12)
                if att:
                    pe.wait_ge(lo_done, m)
                    scores(a, 0)
                project(kacc[0], 0, 0, 12, 24).then_inc(k_done, 1)
                if some(2 * i):
                    pe.wait_ge(v_lo, 2 * i)
                project(vacc[0], 0, 1, 0, 12)
                if att:
                    turn_probs(a, 0, m, 0)
                    scores(a, 1)
                project(vacc[0], 0, 1, 12, 24).then_inc(v_done, 1)
                if att:
                    weigh(a, 0, m)
                if some(2 * i):
                    pe.wait_ge(k_normed, 2 * i)
                project(kacc[1], 1, 0, 0, 12)
                if att:
                    turn_probs(a, 1, m + 1, 1)
                    scores(a, 2)
                    m += 2
                if more:
                    turn_ctx(i, 0, m)
                    m += 2
                project(kacc[1], 1, 0, 12, 24).then_inc(k_done, 1)
                if att:
                    weigh(a, 1, m - (3 if more else 1))
                turn_q(i, 0, m, 0)
                project(vacc[1], 1, 1, 0, 12)
                if att:
                    turn_probs(a, 2, m + 1, 1)
                    scores(a, 3)
                    project(vacc[1], 1, 1, 12, 16)
                    turn_k(i, 0, m + 2, 0)
                    project(vacc[1], 1, 1, 16, 20)
                    turn_k(i, 1, m + 3, 1)
                    project(vacc[1], 1, 1, 20, 24).then_inc(v_done, 1)
                    weigh(a, 2, m + 1)
                    turn_probs(a, 3, m + 4, 0)
                    if more:
                        turn_odd(i, m + 5)
                        turn_q(i, 1, m + 7, 1)
                    else:
                        turn_q(i, 1, m + 5, 1)
                    weigh(a, 3, m + 4)
                else:
                    project(vacc[1], 1, 1, 12, 24).then_inc(v_done, 1)
                    turn_k(i, 0, m + 1, 1)
                    turn_k(i, 1, m + 2, 0)
                    turn_odd(i, m + 3)
                    turn_q(i, 1, m + 5, 1)

            def turn_odd(i, m):
                turn(m, 1, ctx_blocks(1, 0))
                turn(m + 1, 0, ctx_blocks(1, 1))

            iteration(0, M_IT0, att=False)
            iteration(1, M_IT1)
            with pe.Fori(2, 8) as i:
                iteration(i, 12 * i + (M_IT1 - 12))
            for n in (10, 11):
                for g in range(GPU):
                    turn_unit_n(n, g)
            iteration(8, M_IT8)
            with pe.Fori(9, 15) as i:
                iteration(i, 12 * i + (M_IT8 - 96))
            iteration(15, M_IT15, more=False)

            m, w = M_TAIL, 0
            pe.wait_ge(lo_done, M_TAIL)
            pe.wait_ge(v_lo, 32)
            for g in range(4):
                scores(15, g)
                if g:
                    weigh(15, g - 1, m_probs)
                for _ in range(2):
                    if w == 0:
                        pe.wait_ge(raw_loaded[0], raw_count[12])
                    turn(m, m % 2, [raw[:, 0, j, w * P:(w + 1) * P] for j in range(4)])
                    m, w = m + 1, w + 1
                turn_probs(15, g, m, m % 2)
                m_probs = m
                m += 1
            weigh(15, 3, m_probs)

            for n in range(12, 20):
                k = (n - 12) % 4
                pe.wait_ge(lo_done, groups_after(n))
                pe.wait_ge(act_loaded[n % 2], 32 * ((n - 12) // 2 + 1))

                def before(t):
                    if n == 12 and t == 3:
                        pe.wait_ge(o_lo, 64)
                    if k == 0:
                        pe.wait_ge(acc_free, 32 + 4 * ((n - 12) // 4) - 3 + t)

                def after(t, mm):
                    mm.then_inc(acc_done, 1)

                def between(g):
                    turn_unit_n(n + 1, g)
                products(n % 2, lhs_of(n % 2), before, after, k == 0, k == 3, between)

            for t in range(NT):
                pe.wait_ge(ln_done, NT + t + 1)
                for g in range(2):
                    turn(M_LN2 + 2 * t + g, g, [hb[t % 2][:, (4 * g + j) * P:(4 * g + j + 1) * P] for j in range(4)])
            pe.wait_ge(lo_done, M_LN2 + 8)

            tcount = [0]

            def turn_plain(blocks):
                k = tcount[0]
                if some(k - 1):
                    pe.wait_ge(t_read, k - 1)
                for j, src in enumerate(blocks):
                    tr = pe.transpose(ps[:, 6 + k % 2, j * P:(j + 1) * P], src, ident[:])
                tr.then_inc(t_done, 1)
                tcount[0] += 1

            def turn_tile(n, t):
                if n == 20:
                    pe.wait_ge(kv_roped, t + 1)
                    for half in range(2):
                        turn_plain([kr4[:, 4 * half + j].rearrange("p r d -> p (r d)") for j in range(4)])
                else:
                    pe.wait_ge(q_roped, 4 * (n - 21) + t + 1)
                    turn_plain([qr[t % 2][:, j * P:(j + 1) * P] for j in range(4)])

            for n in (20, 21, 22):
                pe.wait_ge(lo_done, groups_before(n) + GPU)

                def before(t):
                    pe.wait_ge(acc_free, 40 + 4 * (n - 20) - 3 + t)

                def after(t, mm):
                    mm.then_inc(acc_done, 1)

                def between(g):
                    if g % 2 == 0 and (n, g) != (20, 0):
                        turn_tile(n if g else n - 1, g // 2 - 1 if g else 3)
                    if n + 1 <= 23:
                        for w in {3: (0,), 4: (1, 2), 5: (3, 4), 6: (5, 6), 7: (7,)}.get(g, ()):
                            turn_unit_n(n + 1, w)
                products(n % 2, lhs_of(0), before, after, between=between)
            turn_tile(22, 3)
            pe.wait_ge(t_read, tcount[0])
            pe.wait_ge(v_doubled, 64)

            def scores2(st):
                pair, gh = divmod(st, 2)
                if some(st):
                    pe.wait_ge(s2_read, st)
                for b2 in range(2):
                    tok = slice(pair * P + b2 * S, pair * P + (b2 + 1) * S)
                    for g in range(4):
                        for h in range(4):
                            rows = slice(DS * h, DS * h + DS)
                            mm = pe.matmul(ps[b2 * S:(b2 + 1) * S, 2 + h, g * S:(g + 1) * S],
                                           q2T[rows, 4 * gh + g, tok], kT4[rows, 4 * gh + g, tok],
                                           start=True, stop=True)
                mm.then_inc(s2_done, 1)

            def weigh2(st):
                pair, gh = divmod(st, 2)
                pe.wait_ge(p2_normed, st + 1)
                for k in range(2):
                    pe.wait_ge(t_read, tcount[0] - 1)
                    for j in range(4):
                        h, mg = 2 * k + j // 2, j % 2
                        tr = pe.transpose(ps[:, k, j * P:(j + 1) * P],
                                          s2[st % 2][:, h * 256 + mg * P:h * 256 + (mg + 1) * P], ident[:])
                    tr.then_inc(t_done, 1)
                    tcount[0] += 1
                pe.wait_ge(t_read, tcount[0])
                if some(st):
                    pe.wait_ge(o2_lo, st)
                for h in range(4):
                    for mg in range(2):
                        for b2 in range(2):
                            for gp in range(2):
                                rows = slice(gp * S, (gp + 1) * S)
                                g = 4 * gh + 2 * mg + gp
                                mm = pe.matmul(ps[DS * h:DS * h + DS, 6 + gp, mg * P + b2 * S:mg * P + (b2 + 1) * S],
                                               vD[rows, 2 * pair + b2, g * DS:(g + 1) * DS],
                                               pT2[rows, h, mg, b2 * S:(b2 + 1) * S], start=True, stop=True)
                mm.then_inc(o2_done, 1)

            pe.wait_ge(lo_done, groups_after(23))
            scores2(0)
            for st in range(8):
                if st < 7:
                    scores2(st + 1)
                weigh2(st)

            pe.wait_ge(w24_loaded, 64)
            for c in range(NC):
                tr = pe.transpose(T[0][:, c * 24:(c + 1) * 24], w24[0:24, c * P:(c + 1) * P], ident[0:24, 0:24])
            tr.then_inc(w24_turned, 1)
            pe.wait_ge(o2_lo, 8)

            def feed(t):
                pe.wait_ge(ln_done, 2 * NT + t + 1)
                for k in range(2):
                    if some(2 * t + k - 1):
                        pe.wait_ge(f_ready, 2 * t + k - 1)
                    for j in range(4):
                        tr = pe.transpose(ps[:, 6 + k, j * P:(j + 1) * P],
                                          z[:, t, (4 * k + j) * P:(4 * k + j + 1) * P], ident[:])
                    tr.then_inc(f_done, 1)
                pe.wait_ge(f_ready, 2 * t + 2)
                if some(t):
                    pe.wait_ge(lg_read, t)
                for c in range(NC):
                    mm = pe.matmul(T[0][:, 0:24], zT[t % 2][:, c, :], w24T[:, c, :],
                                   start=(c == 0), stop=(c == NC - 1))
                mm.then_inc(lg_done, 1)

            for n in (23, 24):
                pe.wait_ge(lo_done, groups_after(n))

                def before(t):
                    pe.wait_ge(acc_free, 52 + 4 * (n - 23) - 3 + t)

                def after(t, mm):
                    mm.then_inc(acc_done, 1)

                def between(g):
                    if n == 23:
                        if g == 4:
                            pe.wait_ge(w24_ready, 1)
                        if g >= 4:
                            for w in (2 * (g - 4), 2 * (g - 4) + 1):
                                turn_unit_n(24, w)
                    elif g % 2 == 1 and g >= 3:
                        feed(g // 2 - 1)
                products(n % 2, lhs_of(1), before, after, between=between)
            feed(3)
            for t in range(NT):
                pe.wait_ge(xp_done, t + 1)
                pe.wait_ge(f_ready, 8 + t)
                for c in range(2):
                    tr = pe.transpose(ps[:, 6, c * P:(c + 1) * P], xp[t % 2][:, c * P:(c + 1) * P], ident[:])
                tr.then_inc(f_done, 1)
                pe.wait_ge(f_ready, 8 + t + 1)
                if some(t):
                    pe.wait_ge(y_scaled, t)
                for c in range(2):
                    mm = pe.matmul(ps[:, 7, 0:CW], xpT[t % 2][:, c, :], wb[:, c, :], start=(c == 0), stop=(c == 1))
                mm.then_inc(y_done, 1)

        def ctx_dst(p, kt, g):
            return ctxT[p][:, 4 * g:4 * g + 4, kt * P:(kt + 1) * P]

        def four(bank):
            return bank.rearrange("p (j n) -> p j n", j=4)

        def wt_dst(slot, p, g):
            return wt[:, slot, p, g, :]

        def ln_dst(p, t, g):
            return act[:, 0, p, :].rearrange("p (c n) -> p c n", c=NC)[:, 4 * g:4 * g + 4, t * P:(t + 1) * P]

        def o2_dst(p, pair, gh, gp):
            c = act[:, 1, p, :].rearrange("p (c n) -> p c n", c=NC)
            return c[:, 4 * gh + gp:4 * gh + gp + 3:2, pair * P:(pair + 1) * P]

        @block.scalar
        def _(sc):
            def hi(m, par, dst, shaped=True, scale=1.0):
                sc.wait_ge(turned, m + 1)
                sc.activation(dst, four(T[par]) if shaped else T[par], ACT.Copy, scale=scale).then_inc(hi_done, 1)

            def hi_unit(n, g):
                hi(groups_before(n) + g, g % 2, wt_dst(n % 2, 0, g), False)

            for m in range(8):
                hi(m, m % 2, ln_dst(0, m // 2, m % 2))
            for g in range(GPU):
                hi_unit(0, g)

            def query_unit(n, par):
                if some(128 * n):
                    sc.wait_ge(q_stored, 128 * n)
                for t in range(NT):
                    hi(M_UNIT0 + GPU + GPU * n + 2 * t, 0, wt_dst(1 - par, 0, 2 * t), False)
                    sc.wait_ge(acc_done, 4 * n + t + 1)
                    sc.activation(qst[t], acc[t], ACT.Copy).then_inc(acc_free, 1)
                    hi(M_UNIT0 + GPU + GPU * n + 2 * t + 1, 1, wt_dst(1 - par, 0, 2 * t + 1), False)

            query_unit(0, 0)
            query_unit(1, 1)
            with sc.Fori(1, 4) as i2:
                query_unit(2 * i2, 0)
                query_unit(2 * i2 + 1, 1)
            for g in range(GPU):
                hi_unit(9, g)
            for kt in range(2):
                for g in range(2):
                    hi(M_CTX0 + 2 * kt + g, g, ctx_dst(0, kt, g))
            sc.wait_ge(wqk_ready, 1)

            def square_k(i, kt):
                sc.wait_ge(k_done, 2 * i + kt + 1)
                if some(2 * i + kt):
                    sc.wait_ge(k_summed, 2 * i + kt)
                sc.activation(sqk, kacc[kt], ACT.Square).then_inc(k_squared, 1)

            def square_q(i):
                sc.wait_ge(qn_loaded, 16 * (i + 1))
                if some(i):
                    sc.wait_ge(q_summed, i)
                sc.activation(sqq, qN, ACT.Square).then_inc(q_squared, 1)

            def exp_s(a, g):
                sc.wait_ge(s_max, 4 * a + g + 1)
                for j in range(2):
                    e = sc.activation(pN[:, j * 256:(j + 1) * 256], sT[:, j * 256:(j + 1) * 256], ACT.Exp,
                                      bias=nmx[:, j:j + 1], accum_out=sm[:, j:j + 1])
                e.then_inc(p_exp, 1)

            def hi_o(a, g):
                sc.wait_ge(o_done, 4 * a + g + 1)
                if some(32 * (2 * a + g // 2)):
                    sc.wait_ge(o_stored[g % 2], 32 * (2 * a + g // 2))
                sc.activation(oS[0][:, g % 2, :], oacc, ACT.Copy).then_inc(o_hi, 1)

            def hi_p(m, par):
                hi(m, par, pT[0], False)

            def hi_k(m, par, kt):
                hi(m, par, kT[0][:, :, kt * P:(kt + 1) * P], scale=wqk)

            def hi_q(m, par, half):
                hi(m, par, qT[0][:, half * 512:(half + 1) * 512], False)

            def hi_v(i):
                sc.wait_ge(v_done, 2 * i + 2)
                if some(4 * i):
                    sc.wait_ge(o_done, 4 * i)
                for kt in range(2):
                    sc.activation(vN[0][:, kt, :], vacc[kt], ACT.Copy).then_inc(v_hi, 1)

            def iteration(i, m, att=True, more=True):
                a = i - 1
                if att:
                    exp_s(a, 0)
                square_k(i, 0)
                if att:
                    hi_p(m, 0)
                    exp_s(a, 1)
                    hi_o(a, 0)
                square_q(i)
                if att:
                    hi_p(m + 1, 1)
                    m += 2
                if more:
                    hi(m, 0, ctx_dst(0, 0, 0))
                    hi(m + 1, 1, ctx_dst(0, 0, 1))
                    m += 2
                if att:
                    exp_s(a, 2)
                    hi_o(a, 1)
                hi_q(m, 0, 0)
                square_k(i, 1)
                if att:
                    hi_p(m + 1, 1)
                    hi_k(m + 2, 0, 0)
                    exp_s(a, 3)
                    hi_k(m + 3, 1, 1)
                    hi_o(a, 2)
                    hi_p(m + 4, 0)
                    if more:
                        hi(m + 5, 1, ctx_dst(0, 1, 0))
                        hi(m + 6, 0, ctx_dst(0, 1, 1))
                        hi_q(m + 7, 1, 1)
                    else:
                        hi_q(m + 5, 1, 1)
                    hi_o(a, 3)
                else:
                    hi_k(m + 1, 1, 0)
                    hi_k(m + 2, 0, 1)
                    hi(m + 3, 1, ctx_dst(0, 1, 0))
                    hi(m + 4, 0, ctx_dst(0, 1, 1))
                    hi_q(m + 5, 1, 1)
                hi_v(i)

            iteration(0, M_IT0, att=False)
            iteration(1, M_IT1)
            with sc.Fori(2, 8) as i:
                iteration(i, 12 * i + (M_IT1 - 12))
            for n in (10, 11):
                for g in range(GPU):
                    hi_unit(n, g)
            iteration(8, M_IT8)
            with sc.Fori(9, 15) as i:
                iteration(i, 12 * i + (M_IT8 - 96))
            iteration(15, M_IT15, more=False)
            m, w = M_TAIL, 0
            for g in range(4):
                if g:
                    hi_o(15, g - 1)
                for _ in range(2):
                    hi(m, m % 2, wt_dst(0, 0, w), False)
                    m, w = m + 1, w + 1
                exp_s(15, g)
                hi_p(m, m % 2)
                m += 1
            hi_o(15, 3)

            for n in range(13, 21):
                for g in range(GPU):
                    hi_unit(n, g)
            for m in range(8):
                hi(M_LN2 + m, m % 2, ln_dst(0, m // 2, m % 2))

            tcount = [0]

            def copy_turned(bank, dst):
                sc.wait_ge(t_done, tcount[0] + 1)
                sc.activation(dst, four(bank), ACT.Copy).then_inc(t_read, 1)
                tcount[0] += 1

            def copy_tile(n, t):
                tok = slice(t * P, (t + 1) * P)
                if n == 20:
                    for half in range(2):
                        copy_turned(ps[:, 6 + tcount[0] % 2, :], kT4[:, 4 * half:4 * half + 4, tok])
                else:
                    u = n - 21
                    copy_turned(ps[:, 6 + tcount[0] % 2, :], q2T[:, 4 * u:4 * u + 4, tok])

            for n in (20, 21, 22):
                for g in range(8):
                    if g % 2 == 0 and (n, g) != (20, 0):
                        copy_tile(n if g else n - 1, g // 2 - 1 if g else 3)
                    for w in {3: (0,), 4: (1, 2), 5: (3, 4), 6: (5, 6), 7: (7,)}.get(g, ()):
                        hi_unit(n + 1, w)
            copy_tile(22, 3)

            def exp2(st):
                sc.wait_ge(s2_ready, st + 1)
                sc.activation(s2[st % 2], s2[st % 2], ACT.Exp).then_inc(p2_exp, 1)

            exp2(0)
            for st in range(8):
                pair, gh = divmod(st, 2)
                if st < 7:
                    exp2(st + 1)
                for k in range(2):
                    copy_turned(ps[:, k, :], pT2[:, 2 * k:2 * k + 2, :, :].rearrange("p h m n -> p (h m) n"))
                sc.wait_ge(o2_done, st + 1)
                for gp in range(2):
                    o = sc.activation(o2_dst(0, pair, gh, gp), ps[:, 6 + gp, 0:256].rearrange("p (m n) -> p m n", m=2),
                                      ACT.Copy)
                o.then_inc(o2_hi, 1)

            sc.wait_ge(w24_turned, 1)
            sc.activation(w24T, T[0][:, 0:192].rearrange("p (c n) -> p c n", c=NC), ACT.Copy).then_inc(w24_ready, 1)
            for w in range(GPU):
                hi_unit(24, w)
            sc.wait_ge(const_loaded, 144)
            sc.activation(gts[:, 1:2], gts[:, 0:1], ACT.Exp, scale=-1.0).then_inc(sk_out, 1)
            for t in range(NT):
                sc.wait_ge(ln_done, 2 * NT + t + 1)
                sc.activation(zsq, z[:, t, :], ACT.Square, accum_out=ssz[:, t:t + 1]).then_inc(z_squared, 1)
                for k in range(2):
                    sc.wait_ge(f_done, 2 * t + k + 1)
                    if k == 0:
                        if some(t - 1):
                            sc.wait_ge(lg_done, t - 1)
                    sc.activation(zT[t % 2][:, 4 * k:4 * k + 4, :], four(ps[:, 6 + k, :]), ACT.Copy
                                  ).then_inc(f_ready, 1)

            asked = [0]

            def answer(dst, src, func):
                asked[0] += 1
                sc.wait_ge(sk_in, asked[0])
                sc.activation(dst, src, func).then_inc(sk_out, 1)

            def branch(t):
                sc.wait_ge(f_done, 8 + t + 1)
                sc.activation(xpT[t % 2], ps[:, 6, 0:256].rearrange("p (c n) -> p c n", c=2), ACT.Copy
                              ).then_inc(f_ready, 1)
                sc.wait_ge(y_done, t + 1)
                for i in range(NSTR):
                    c = 8 * t + 4 + i
                    y = sc.activation(yS[:, t, i * CW:(i + 1) * CW], ps[:, 7, 0:CW], ACT.Copy, scale=h8[:, c:c + 1])
                y.then_inc(y_scaled, 1)

            answer(h8, h8, ACT.Exp)
            for src, func in ((A, ACT.Exp), (uv[:, 0:16], ACT.Ln), (A, ACT.Exp), (uv[:, 0:16], ACT.Ln), (A, ACT.Exp)):
                answer(Kx if func == ACT.Exp else luv[:, 0:16], src, func)
            for e in range(4):
                branch(e)
                answer(luv, uv, ACT.Ln)
                answer(Kx, A, ACT.Exp)

        @block.vector
        def _(v):
            given, open_ = {acc_free: 32}, set()

            def done(ins, signal=dv):
                given[signal] = given.get(signal, 0) + 1
                open_.add(signal)
                return ins.then_inc(signal, 1)

            def settle():
                for signal in sorted(open_, key=lambda y: y.name):
                    v.wait_ge(signal, given[signal])
                open_.clear()

            def lo(m, par, dst, hi_, shaped=True):
                v.wait_ge(hi_done, m + 1)
                v.tensor_tensor(dst, four(T[par]) if shaped else T[par], hi_.bitcast(F32), ALU.subtract
                                ).then_inc(lo_done, 1)

            def lo_unit(n, g):
                lo(groups_before(n) + g, g % 2, wt_dst(n % 2, 1, g), wt_dst(n % 2, 0, g), False)

            def stats(t, eps=EPS):
                for h in range(2):
                    done(v.bn_stats(bst[:, 6 * h:6 * h + 6], xr[:, t, h * 512:(h + 1) * 512]))
                settle()
                done(v.bn_aggr(bag[:, 2 * t:2 * t + 2], bst))
                settle()
                v.tensor_scalar(lnv[:, t:t + 1], bag[:, 2 * t + 1:2 * t + 2], eps, None, ALU.add).then_inc(ln_var, 1)

            def normalise(k, t, dst):
                v.wait_ge(ln_rstd, k + 1)
                v.tensor_scalar(dst, xr[:, t, :], bag[:, 2 * t:2 * t + 1], lnr[:, t:t + 1],
                                ALU.subtract, ALU.mult).then_inc(ln_done, 1)

            def ln_lo(m0, t):
                for g in range(2):
                    lo(m0 + 2 * t + g, g, ln_dst(1, t, g), ln_dst(0, t, g))

            v.wait_ge(x_loaded, 16)
            for t in range(NT):
                stats(t)
            normalise(0, 0, hb[0])
            normalise(1, 1, hb[1])
            ln_lo(0, 0)
            normalise(2, 2, hb[0])
            ln_lo(0, 1)
            normalise(3, 3, hb[1])
            ln_lo(0, 2)
            ln_lo(0, 3)
            for g in range(GPU):
                lo_unit(0, g)

            def query_unit(n, par):
                for g in range(GPU):
                    lo(M_UNIT0 + GPU + GPU * n + g, g % 2, wt_dst(1 - par, 1, g), wt_dst(1 - par, 0, g), False)

            query_unit(0, 0)
            query_unit(1, 1)
            with v.Fori(1, 4) as i2:
                query_unit(2 * i2, 0)
                query_unit(2 * i2 + 1, 1)
            for g in range(GPU):
                lo_unit(9, g)
            v.wait_ge(const_loaded, 144)
            v.scalar_tensor_tensor(wqk, qw, float(DH) ** 0.5, kw, ALU.mult, ALU.mult).then_inc(wqk_ready, 1)
            for kt in range(2):
                for g in range(2):
                    lo(M_CTX0 + 2 * kt + g, g, ctx_dst(1, kt, g), ctx_dst(0, kt, g))
            v.wait_ge(wqk_ready, 1)
            v.wait_ge(mask_loaded, 32)

            def read_scores(a, g):
                if g == 0:
                    v.wait_ge(q_rstd, a + 1)
                v.wait_ge(s_done, 4 * a + g + 1)
                for j in range(2):
                    r = v.scalar_tensor_tensor(sT[:, j * 256:(j + 1) * 256], sacc[:, j * 256:(j + 1) * 256],
                                               rq[:, 2 * g + j:2 * g + j + 1], mask2, ALU.mult, ALU.add)
                r.then_inc(s_read, 1)
                v.wait_ge(s_read, 4 * a + g + 1)
                v.tensor_reduce(nmx[:, 0:2], sT.rearrange("p (j n) -> p j n", j=2), AX, ALU.max, negate=True
                                ).then_inc(s_max, 1)

            def norm_probs(a, g):
                v.wait_ge(p_exp, 4 * a + g + 1)
                v.reciprocal(rsm[:, 0:2], sm[:, 0:2]).then_inc(sum_inverted, 1)
                v.wait_ge(sum_inverted, 4 * a + g + 1)
                for j in range(2):
                    r = v.tensor_scalar(pN[:, j * 256:(j + 1) * 256], pN[:, j * 256:(j + 1) * 256],
                                        rsm[:, j:j + 1], None, ALU.mult)
                r.then_inc(p_normed, 1)

            def sum_k(i, kt):
                v.wait_ge(k_squared, 2 * i + kt + 1)
                if some(2 * i + kt):
                    v.wait_ge(k_var, 2 * i + kt)
                v.tensor_reduce(ssk, sqk.rearrange("p (g d) -> p g d", g=4), AX, ALU.add).then_inc(k_summed, 1)

            def norm_k(i, kt):
                v.wait_ge(k_rstd, 2 * i + kt + 1)
                v.tensor_tensor(kn[kt].rearrange("p (g d) -> p g d", g=4),
                                kacc[kt].rearrange("p (g d) -> p g d", g=4),
                                rk.unsqueeze(2).broadcast_to([P, 4, DH]), ALU.mult).then_inc(k_normed, 1)

            def sum_q(i):
                v.wait_ge(q_squared, i + 1)
                if some(i):
                    v.wait_ge(q_var, i)
                v.tensor_reduce(ssq, sqq.rearrange("p (g d) -> p g d", g=8), AX, ALU.add).then_inc(q_summed, 1)

            def lo_o(a, g):
                v.wait_ge(o_hi, 4 * a + g + 1)
                v.tensor_tensor(oS[1][:, g % 2, :], oacc, oS[0][:, g % 2, :].bitcast(F32), ALU.subtract
                                ).then_inc(o_lo, 1)

            def lo_p(m, par):
                lo(m, par, pT[1], pT[0], False)

            def lo_k(m, par, kt):
                v.wait_ge(hi_done, m + 1)
                hi_, dst = (kT[p][:, :, kt * P:(kt + 1) * P] for p in range(2))
                v.scalar_tensor_tensor(dst, four(T[par]), wqk, hi_.bitcast(F32), ALU.mult, ALU.subtract
                                       ).then_inc(lo_done, 1)

            def lo_q(m, par, half):
                hi_, dst = (qT[p][:, half * 512:(half + 1) * 512] for p in range(2))
                lo(m, par, dst, hi_, False)

            def lo_ctx(m, par, kt, g):
                lo(m, par, ctx_dst(1, kt, g), ctx_dst(0, kt, g))

            def lo_v(i):
                for kt in range(2):
                    v.wait_ge(v_hi, 2 * i + kt + 1)
                    v.tensor_tensor(vN[1][:, kt, :], vacc[kt], vN[0][:, kt, :].bitcast(F32), ALU.subtract
                                    ).then_inc(v_lo, 1)

            def iteration(i, m, att=True, more=True):
                a = i - 1
                if att:
                    read_scores(a, 0)
                    norm_probs(a, 0)
                sum_k(i, 0)
                if att:
                    lo_p(m, 0)
                    read_scores(a, 1)
                norm_k(i, 0)
                if att:
                    norm_probs(a, 1)
                    lo_o(a, 0)
                sum_q(i)
                if att:
                    lo_p(m + 1, 1)
                    read_scores(a, 2)
                    m += 2
                if more:
                    lo_ctx(m, 0, 0, 0)
                    lo_ctx(m + 1, 1, 0, 1)
                    m += 2
                if att:
                    norm_probs(a, 2)
                    lo_o(a, 1)
                lo_q(m, 0, 0)
                sum_k(i, 1)
                if att:
                    lo_p(m + 1, 1)
                    norm_k(i, 1)
                    read_scores(a, 3)
                    lo_k(m + 2, 0, 0)
                    norm_probs(a, 3)
                    lo_k(m + 3, 1, 1)
                    lo_o(a, 2)
                    lo_p(m + 4, 0)
                    if more:
                        lo_ctx(m + 5, 1, 1, 0)
                        lo_ctx(m + 6, 0, 1, 1)
                        lo_q(m + 7, 1, 1)
                    else:
                        lo_q(m + 5, 1, 1)
                    lo_o(a, 3)
                else:
                    norm_k(i, 1)
                    lo_k(m + 1, 1, 0)
                    lo_k(m + 2, 0, 1)
                    lo_ctx(m + 3, 1, 1, 0)
                    lo_ctx(m + 4, 0, 1, 1)
                    lo_q(m + 5, 1, 1)
                lo_v(i)

            iteration(0, M_IT0, att=False)
            iteration(1, M_IT1)
            with v.Fori(2, 8) as i:
                iteration(i, 12 * i + (M_IT1 - 12))
            for n in (10, 11):
                for g in range(GPU):
                    lo_unit(n, g)
            iteration(8, M_IT8)
            with v.Fori(9, 15) as i:
                iteration(i, 12 * i + (M_IT8 - 96))
            iteration(15, M_IT15, more=False)
            m, w = M_TAIL, 0
            for g in range(4):
                read_scores(15, g)
                if g:
                    lo_o(15, g - 1)
                for _ in range(2):
                    lo(m, m % 2, wt_dst(0, 1, w), wt_dst(0, 0, w), False)
                    m, w = m + 1, w + 1
                norm_probs(15, g)
                lo_p(m, m % 2)
                m += 1
            lo_o(15, 3)

            def add_tile(count, t, half):
                v.wait_ge(acc_done, count)
                s = xr[:, t, half * UW:(half + 1) * UW]
                done(v.tensor_tensor(s, acc[t], s, ALU.add), acc_free)

            for n in range(12, 20):
                k, o = (n - 12) % 4, (n - 12) // 4
                for t in range(NT):
                    lo_unit(n + 1, 2 * t)
                    if k == 3:
                        if n == 15 and t == 0:
                            v.wait_ge(x_loaded, 32)
                        add_tile(32 + 4 * (n - 12) + t + 1, t, o)
                    lo_unit(n + 1, 2 * t + 1)
                    if n == 19:
                        settle()
                        stats(t)
                        if t < 2:
                            normalise(NT + t, t, hb[t])
            ln_lo(M_LN2, 0)
            normalise(NT + 2, 2, hb[0])
            ln_lo(M_LN2, 1)
            normalise(NT + 3, 3, hb[1])
            ln_lo(M_LN2, 2)
            ln_lo(M_LN2, 3)

            def rotate(src, d, t, nh):
                s3, d3, t3 = (y.rearrange("p (h d) -> p h d", d=DS) for y in (src, d, t))
                half = DS // 2

                def table(tab, a, b):
                    return tab[:, a:b].unsqueeze(1).broadcast_to([P, nh, b - a])
                settle()
                done(v.tensor_tensor(d3, s3, table(cosb, 0, DS), ALU.mult))
                done(v.tensor_tensor(t3[:, :, 0:half], s3[:, :, half:DS], table(sinb, 0, half), ALU.mult))
                done(v.tensor_tensor(t3[:, :, half:DS], s3[:, :, 0:half], table(sinb, half, DS), ALU.mult), acc_free)

            def rotate_tile(n, t):
                v.wait_ge(acc_done, 64 + 4 * (n - 20) + t + 1)
                if n == 20:
                    done(v.tensor_copy(vS[:, t, :], acc[t][:, 256:512]))
                    rotate(acc[t][:, 0:256], t2[:, 0:256], t2[:, 256:512], 8)
                    settle()
                    if some(2 * t):
                        v.wait_ge(t_done, 2 * t)
                    d3, t3 = (y.rearrange("p (g d) -> p g d", d=DS).unsqueeze(2).broadcast_to([P, 8, 4, DS])
                              for y in (t2[:, 0:256], t2[:, 256:512]))
                    done(v.tensor_tensor(kr4, d3, t3, ALU.add), kv_roped)
                else:
                    u = 4 * (n - 21) + t
                    v.wait_ge(t_done, 8 if u < 2 else 7 + u)
                    rotate(acc[t], qr[t % 2], t2, 16)
                    settle()
                    done(v.tensor_tensor(qr[t % 2], qr[t % 2], t2, ALU.add), q_roped)

            for n in (20, 21, 22):
                for g in range(8):
                    if g % 2 == 1:
                        rotate_tile(n, g // 2)
                    for w in {3: (0,), 4: (1, 2), 5: (3, 4), 6: (5, 6), 7: (7,)}.get(g, ()):
                        lo_unit(n + 1, w)

            def tiles16(y):
                return y.rearrange("p (h k) -> p h k", h=16)

            def each(y):
                return y[:, 0:16].unsqueeze(2).broadcast_to([P, 16, S])

            def read_scores2(st):
                v.wait_ge(s2_done, st + 1)
                y = s2[st % 2]
                done(v.scalar_tensor_tensor(y.rearrange("p (h n) -> p h n", h=4), ps[:, 2:6, 0:256],
                                            float(DS) ** -0.5, cmask.unsqueeze(1).broadcast_to([P, 4, 256]),
                                            ALU.mult, ALU.add), s2_read)
                settle()
                done(v.tensor_reduce(nmx, tiles16(y), AX, ALU.max))
                settle()
                done(v.tensor_tensor(tiles16(y), tiles16(y), each(nmx), ALU.subtract), s2_ready)

            def norm_probs2(st):
                v.wait_ge(p2_exp, st + 1)
                y = s2[st % 2]
                done(v.tensor_reduce(sm, tiles16(y), AX, ALU.add))
                settle()
                done(v.reciprocal(rsm, sm))
                settle()
                done(v.tensor_tensor(tiles16(y), tiles16(y), each(rsm), ALU.mult), p2_normed)

            def lo_o2(st):
                pair, gh = divmod(st, 2)
                v.wait_ge(o2_hi, st + 1)
                for gp in range(2):
                    r = v.tensor_tensor(o2_dst(1, pair, gh, gp), ps[:, 6 + gp, 0:256].rearrange("p (m n) -> p m n", m=2),
                                        o2_dst(0, pair, gh, gp).bitcast(F32), ALU.subtract)
                r.then_inc(o2_lo, 1)

            read_scores2(0)
            for st in range(8):
                if st < 7:
                    read_scores2(st + 1)
                norm_probs2(st)
                if st:
                    lo_o2(st - 1)
            lo_o2(7)

            for t in range(2):
                add_tile(76 + t + 1, t, 0)
            lo_unit(24, 0)
            lo_unit(24, 1)
            add_tile(76 + 3, 2, 0)
            for w in range(2, 6):
                lo_unit(24, w)
            add_tile(76 + 4, 3, 0)
            lo_unit(24, 6)
            lo_unit(24, 7)

            def logits(t):
                v.wait_ge(lg_done, t + 1)
                v.wait_ge(z_rstd, t + 1)
                done(v.scalar_tensor_tensor(L[:, t, :], T[0][:, 0:24], rz[:, t:t + 1], base24, ALU.mult, ALU.add),
                     lg_read)

            for t in range(NT):
                add_tile(80 + t + 1, t, 1)
                settle()
                stats(t)
                normalise(2 * NT + t, t, z[:, t, :])
                if t >= 2:
                    logits(t - 2)
            logits(2)
            logits(3)
            settle()

            n8 = L[:, :, 16:24].rearrange("p t (s k) -> p t s k", s=2)
            h84 = h8.rearrange("p (t s k) -> p t s k", t=NT, s=2)
            h8r = h8.rearrange("p (n k) -> p n k", k=NSTR)
            done(v.tensor_reduce(h8m, n8, AX, ALU.max))
            settle()
            done(v.tensor_tensor(h84, n8, h8m.rearrange("p (t s) -> p t s", t=NT).unsqueeze(3)
                                 .broadcast_to([P, NT, 2, NSTR]), ALU.subtract), sk_in)
            done(v.tensor_scalar(A.rearrange("p (t n) -> p t n", t=NT), L[:, :, 0:16], TAU_INV, None, ALU.mult))
            answers = [2]

            def by_rows(y):
                return y.rearrange("p (n j) -> p n j", j=NSTR)

            def by_cols(y):
                return y.rearrange("p (t i j) -> p t j i", t=NT, i=NSTR)

            def sums_cols(y):
                return y.rearrange("p (t j) -> p t j", t=NT)

            def over_rows(y):
                return y.unsqueeze(2).broadcast_to([P, 16, NSTR])

            def over_cols(y):
                return sums_cols(y).unsqueeze(3).broadcast_to([P, NT, NSTR, NSTR])

            for view, over in ((by_rows, over_rows), (by_cols, over_cols)):
                sums = (lambda y: y) if view is by_rows else sums_cols
                settle()
                done(v.tensor_reduce(sums(nmx), view(A), AX, ALU.max))
                settle()
                done(v.tensor_tensor(view(A), view(A), over(nmx), ALU.subtract), sk_in)
                v.wait_ge(sk_out, answers[0] + 1)
                done(v.tensor_reduce(sums(uv[:, 0:16]), view(Kx), AX, ALU.add), sk_in)
                v.wait_ge(sk_out, answers[0] + 2)
                settle()
                done(v.tensor_tensor(view(A), view(A), over(luv[:, 0:16]), ALU.subtract),
                     dv if view is by_rows else sk_in)
                answers[0] += 2
            answers[0] += 1

            done(v.tensor_reduce(h8s, h8r, AX, ALU.add))
            settle()
            done(v.reciprocal(h8m, h8s))
            settle()
            done(v.tensor_tensor(h8r, h8r, h8m.unsqueeze(2).broadcast_to([P, 8, NSTR]), ALU.mult), mix_ready)
            done(v.tensor_scalar(gts[:, 1:2], gts[:, 1:2], 1.0, None, ALU.add))
            settle()
            done(v.reciprocal(gts[:, 2:3], gts[:, 1:2]))
            settle()
            done(v.tensor_scalar(gts[:, 3:4], gts[:, 2:3], -1.0, 1.0, ALU.mult, ALU.add))

            ua, ub = uv[:, 0:16], uv[:, 16:32]
            tr_, tc_ = by_rows(tk), by_cols(tk)
            for epoch in range(ITERS // EPOCH):
                if epoch:
                    v.wait_ge(sk_out, answers[0] + 1)
                    done(v.tensor_tensor(by_rows(A), by_rows(A), over_rows(luv[:, 0:16]), ALU.add))
                    settle()
                    done(v.tensor_tensor(by_cols(A), by_cols(A), over_cols(luv[:, 16:32]), ALU.add), sk_in)
                    answers[0] += 2
                v.wait_ge(sk_out, answers[0])
                for it in range(1 if epoch == 0 else 0, EPOCH):
                    first = it == (1 if epoch == 0 else 0)
                    if not first:
                        done(v.tensor_tensor(tc_, by_cols(Kx), over_cols(ub), ALU.mult))
                        settle()
                    done(v.tensor_reduce(ua, by_rows(Kx if first else tk), AX, ALU.add))
                    settle()
                    done(v.reciprocal(ua, ua))
                    settle()
                    done(v.tensor_tensor(tr_, by_rows(Kx), over_rows(ua), ALU.mult))
                    settle()
                    done(v.tensor_reduce(sums_cols(ub), tc_, AX, ALU.add))
                    settle()
                    last = it == EPOCH - 1 and epoch < ITERS // EPOCH - 1
                    done(v.reciprocal(ub, ub), sk_in if last else dv)
                    settle()
            done(v.tensor_tensor(tc_, tc_, over_cols(ub), ALU.mult))
            settle()
            done(v.tensor_scalar(hres, tk, gts[:, 2:3], None, ALU.mult))
            settle()
            diag = hres.rearrange("p (t n) -> p t n", t=NT)[:, :, 0:16:5]
            done(v.tensor_scalar(diag, diag, gts[:, 3:4], None, ALU.add))
            settle()
            for t in range(NT):
                v.wait_ge(y_added, t + 1)
                for j in range(NSTR):
                    settle()
                    for i in range(NSTR):
                        c = 16 * t + 4 * i + j
                        o = xr[:, t, i * CW:(i + 1) * CW]
                        done(v.scalar_tensor_tensor(o, z[:, t, j * CW:(j + 1) * CW], hres[:, c:c + 1], o,
                                                    ALU.mult, ALU.add),
                             out_ready if (i, j) == (NSTR - 1, NSTR - 1) else dv)

        @block.gpsimd
        def _(pool):
            pool.memset(mhalf, -0.5).then_inc(mhalf_ready, 1)
            pool.memset(epsd, DH * EPS).then_inc(mhalf_ready, 1)
            pool.wait_ge(mhalf_ready, 2)

            def root(dst, src, n, signals):
                pool.tensor_tensor(dst, src, mhalf[:, 0:n], ALU.pow).then_inc(signals, 1)

            def ln_root(k):
                pool.wait_ge(ln_var, k + 1)
                root(lnr[:, k % NT:k % NT + 1], lnv[:, k % NT:k % NT + 1], 1, ln_rstd)

            for k in range(NT):
                ln_root(k)

            def k_root(i, kt):
                pool.wait_ge(k_summed, 2 * i + kt + 1)
                pool.tensor_tensor(msk, ssk, epsd[:, 0:4], ALU.add).then_inc(k_var, 1)
                pool.wait_ge(k_var, 2 * i + kt + 1)
                if some(2 * i + kt):
                    pool.wait_ge(k_normed, 2 * i + kt)
                root(rk, msk, 4, k_rstd)

            def iteration(i):
                k_root(i, 0)
                pool.wait_ge(q_summed, i + 1)
                pool.tensor_tensor(msq, ssq, epsd, ALU.add).then_inc(q_var, 1)
                k_root(i, 1)
                pool.wait_ge(q_var, i + 1)
                if some(4 * i):
                    pool.wait_ge(s_read, 4 * i)
                root(rq, msq, 8, q_rstd)

            iteration(0)
            with pool.Fori(1, 16) as i:
                iteration(i)
            for k in range(NT, 3 * NT):
                ln_root(k)
                if k >= 2 * NT:
                    t = k - 2 * NT
                    pool.wait_ge(z_squared, t + 1)
                    pool.tensor_scalar(msz[:, t:t + 1], ssz[:, t:t + 1], 1.0 / E, EPS_FFN, ALU.mult, ALU.add
                                       ).then_inc(z_var, 1)
                    pool.wait_ge(z_var, t + 1)
                    root(rz[:, t:t + 1], msz[:, t:t + 1], 1, z_rstd)

            pool.wait_ge(mix_ready, 1)
            n = 0
            for t in range(NT):
                pool.wait_ge(f_done, 8 + t - 1)
                for j in range(NSTR):
                    zj, w = z[:, t, j * CW:(j + 1) * CW], h8[:, 8 * t + j:8 * t + j + 1]
                    dst = xp[t % 2] if j == 0 else zsq[:, 0:CW]
                    pool.tensor_scalar(dst, zj, w, None, ALU.mult).then_inc(pl, 1)
                    n += 1
                    pool.wait_ge(pl, n)
                    if j == 0:
                        continue
                    add = pool.tensor_tensor(xp[t % 2], xp[t % 2], zsq[:, 0:CW], ALU.add)
                    if j < NSTR - 1:
                        add.then_inc(pl, 1)
                        n += 1
                        pool.wait_ge(pl, n)
                    else:
                        add.then_inc(xp_done, 1)
                        pool.wait_ge(xp_done, t + 1)
            for t in range(NT):
                pool.wait_ge(y_scaled, t + 1)
                pool.tensor_tensor(xr[:, t, :], xr[:, t, :], yS[:, t, :], ALU.add).then_inc(y_added, 1)


_INS = ["x", "ctx_4096", "mask_1x1xSxS2_ff0", "L0_xattn_q_proj_w", "L0_xattn_k_proj_w", "L0_xattn_v_proj_w",
        "L0_xattn_o_proj_w", "L0_xattn_q_norm_w", "L0_xattn_k_norm_w", "L0_attn_Wq", "L0_attn_Wk", "L0_attn_Wv",
        "L0_attn_Wo", "L0_ffn_W_res", "L0_ffn_W_pre", "L0_ffn_W_post", "L0_ffn_H_res_base", "L0_ffn_H_pre_base",
        "L0_ffn_H_post_base", "L0_ffn_gate", "L0_ffn_W_branch"]


def _constants(np):
    f = np.float32
    inv = (f(1.0) / f(500000.0) ** (np.arange(0, DS, 2, dtype=f) / f(DS))).astype(f)
    wave = (f(2.0 * np.pi) / inv).astype(f)
    factor, hi_f, lo_f, orig = f(32.0), 4.0, 1.0, 2048
    low = np.where(wave > orig / lo_f, inv / factor, inv).astype(f)
    smooth = ((orig / wave - f(lo_f)) / f(hi_f - lo_f)).astype(f)
    smoothed = ((1 - smooth) * low / factor + smooth * low).astype(f)
    medium = ~(wave < orig / lo_f) & ~(wave > orig / hi_f)
    inv = np.where(medium, smoothed, low).astype(f)
    ang = np.arange(S, dtype=f)[:, None] * inv[None, :]
    cos, sin = np.cos(ang).astype(f), np.sin(ang).astype(f)
    cos = np.tile(np.concatenate([cos, cos], 1), (2, 1))
    sin = np.tile(np.concatenate([-sin, sin], 1), (2, 1))
    causal = np.where(np.tril(np.ones((S, S), bool)), f(0.0), f(-3.0e38)).astype(f)
    return {"ident": np.eye(P, dtype=f), "cos": cos, "sin": sin, "causal": np.tile(causal, (2, 4))}


def kernel(**inputs):
    import numpy as np
    import concourse.bacc as bacc
    from concourse.bass_utils import run_bass_kernel_spmd

    nc = bacc.Bacc("TRN2", target_bir_lowering=False, num_devices=1)
    arrays = {f"in_{name}": np.ascontiguousarray(inputs[name]) for name in _INS}
    arrays.update({f"const_{k}": np.ascontiguousarray(v) for k, v in _constants(np).items()})
    args = [nc.dram_tensor(name, a.shape, F32, kind="ExternalInput").ap() for name, a in arrays.items()]
    q_rows = nc.dram_tensor("q_rows", (2, 2, B, S, 4, 2, DH), F32, kind="Internal").ap()
    ot = [nc.dram_tensor(f"ot_{p}", (P, 2, 16, B, S), F32, kind="Internal").ap() for p in ("hi", "lo")]
    out = nc.dram_tensor("out", (B, S, E), F32, kind="ExternalOutput").ap()
    perceiver(nc, *args, q_rows, *ot, out)
    return run_bass_kernel_spmd(nc, [arrays], core_ids=[0]).results[0]["out"]
```
